# Optimizing a Trainium2 kernel written in Bass

```python
import numpy as np
import jax
import jax.numpy as jnp

def _softmax(x, axis=-1):
    return jax.nn.softmax(x, axis=axis)

def _gelu(x):
    return jax.nn.gelu(x, approximate=True)

def _silu(x):
    return jax.nn.silu(x)

def _sigmoid(x):
    return jax.nn.sigmoid(x)

def _layernorm(x, axis=-1, eps=1e-05):
    m = jnp.mean(x, axis=axis, keepdims=True)
    v = jnp.var(x, axis=axis, keepdims=True)
    return (x - m) / jnp.sqrt(v + eps)

def _scatter_add(tgt, idx, src, axis=0):
    return tgt.at[idx].add(src)

def _segment_sum(src, seg, n):
    return jax.ops.segment_sum(src, seg, n)
kernel_name = 'mk_gnn_resnorm_d4_gnn_r8_308524'

def setup_inputs(seed: int=0):
    np.random.seed(seed)
    _w = jnp.asarray

    def _rec_inputs():
        import jax
        import jax.numpy as jnp
        _gk = jax.random.key(seed)
        x = -0.000202 + 1 * jax.random.normal(jax.random.fold_in(_gk, 1), (6250, 64), jnp.float32)
        src = jax.random.randint(jax.random.fold_in(_gk, 2), (200000,), 0, 6250, jnp.int32)
        dst = jnp.minimum((6250 * jax.random.uniform(jax.random.fold_in(_gk, 3), (200000,)) ** 2.0).astype(jnp.int32), 49999)
        _o = jnp.argsort(dst, stable=True)
        src = src[_o]
        dst = dst[_o]
        edge_attr_128 = jax.random.uniform(jax.random.fold_in(_gk, 12), (200000, 128), jnp.float32, 0.0, 1)
        edge_attr_16 = -0.00010739 + 0.99994 * jax.random.normal(jax.random.fold_in(_gk, 13), (200000, 16), jnp.float32)
        edge_attr_64 = -8.16379e-05 + 0.999858 * jax.random.normal(jax.random.fold_in(_gk, 14), (200000, 64), jnp.float32)
        edge_type_3 = jax.random.randint(jax.random.fold_in(_gk, 16), (200000,), 0, 3, jnp.int32)
        node_type_2 = jax.random.randint(jax.random.fold_in(_gk, 17), (6250,), 0, 2, jnp.int32)
        return (x, src, dst, edge_attr_128, edge_attr_16, edge_attr_64, edge_type_3, node_type_2)
    x, src, dst, edge_attr_128, edge_attr_16, edge_attr_64, edge_type_3, node_type_2 = _rec_inputs()

    def _L0_gnn_setup():
        import jax, jax.numpy as jnp
        import numpy as np
        N, M = (12500, 100000)
        F_IN, F_E, H = (64, 16, 64)
        T_NODE, T_EDGE = (2, 3)
        HEAD_DIM = 16.0

        def _node_proj(x, W, b, node_type):
            p = jnp.einsum('nf,tfh->tnh', x, W) + b[:, None, :]
            return jnp.take_along_axis(p, node_type[None, :, None], axis=0)[0]
        key = jax.random.key(seed)
        ks = jax.random.split(key, 16)
        inp = {'x': jax.random.normal(ks[0], (N, F_IN), jnp.float32), 'edge_feat': jax.random.normal(ks[1], (M, F_E), jnp.float32), 'node_type': jax.random.randint(ks[2], (N,), 0, T_NODE, jnp.int32), 'edge_src': jax.random.randint(ks[3], (M,), 0, N, jnp.int32), 'edge_dst': jax.random.randint(ks[4], (M,), 0, N, jnp.int32), 'edge_type': jax.random.randint(ks[5], (M,), 0, T_EDGE, jnp.int32)}
        s_n = 1.0 / np.sqrt(F_IN)
        s_e = 1.0 / np.sqrt(F_E)
        for i, name in enumerate(['W1', 'W2', 'W3', 'W4']):
            inp[name] = jax.random.normal(ks[6 + i], (T_NODE, F_IN, H), jnp.float32) * s_n
            inp['b' + name[1]] = jax.random.normal(ks[10 + i], (T_NODE, H), jnp.float32) * 0.01
        inp['W5'] = jax.random.normal(ks[14], (T_EDGE, F_E, H), jnp.float32) * s_e
        inp['b5'] = jax.random.normal(ks[15], (T_EDGE, H), jnp.float32) * 0.01
        return inp
    _L0_gnn_all = _L0_gnn_setup()
    _L0_gnn_in = {k: v for k, v in _L0_gnn_all.items() if k in ('W1', 'b1', 'W2', 'b2', 'W3', 'b3', 'W4', 'b4', 'W5', 'b5')}
    del _L0_gnn_all

    def _L1_gnn_setup():
        import jax, jax.numpy as jnp
        import numpy as np
        N_NODES = 12500
        N_EDGES = 156250
        D_IN = 64
        D_HID = 64
        D_OUT = 64

        def sage_conv(x, edge_index, w_l, b_l, w_r):
            src, dst = (edge_index[0], edge_index[1])
            n = x.shape[0]
            msg_sum = jax.ops.segment_sum(x[src], dst, num_segments=n)
            deg = jax.ops.segment_sum(jnp.ones((src.shape[0],), x.dtype), dst, num_segments=n)
            mean = msg_sum / jnp.maximum(deg, 1.0)[:, None]
            return mean @ w_l + b_l + x @ w_r
        key = jax.random.key(seed)
        ks = jax.random.split(key, 8)
        x = jax.random.normal(ks[0], (N_NODES, D_IN), dtype=jnp.float32)
        edge_index = jax.random.randint(ks[1], (2, N_EDGES), 0, N_NODES, dtype=jnp.int64)
        s1 = 1.0 / np.sqrt(D_IN)
        s2 = 1.0 / np.sqrt(D_HID)
        w1_l = jax.random.uniform(ks[2], (D_IN, D_HID), jnp.float32, -s1, s1)
        w1_r = jax.random.uniform(ks[3], (D_IN, D_HID), jnp.float32, -s1, s1)
        b1 = jax.random.uniform(ks[4], (D_HID,), jnp.float32, -s1, s1)
        w2_l = jax.random.uniform(ks[5], (D_HID, D_OUT), jnp.float32, -s2, s2)
        w2_r = jax.random.uniform(ks[6], (D_HID, D_OUT), jnp.float32, -s2, s2)
        b2 = jax.random.uniform(ks[7], (D_OUT,), jnp.float32, -s2, s2)
        return {'x': x, 'edge_index': edge_index, 'w1_l': w1_l, 'b1': b1, 'w1_r': w1_r, 'w2_l': w2_l, 'b2': b2, 'w2_r': w2_r}
    _L1_gnn_all = _L1_gnn_setup()
    _L1_gnn_in = {k: v for k, v in _L1_gnn_all.items() if k in ('w1_l', 'b1', 'w1_r', 'w2_l', 'b2', 'w2_r')}
    del _L1_gnn_all

    def _L2_gnn_setup():
        import jax, jax.numpy as jnp
        import numpy as np
        N_NODES = 12500
        N_EDGES = 125000
        D_IN = 64
        EDGE_DIM = 16
        D_OUT = 64
        key = jax.random.key(seed)
        ks = jax.random.split(key, 8)
        x = jax.random.normal(ks[0], (N_NODES, D_IN), dtype=jnp.float32)
        edge_attr = jax.random.normal(ks[1], (N_EDGES, EDGE_DIM), dtype=jnp.float32)
        W_e = jax.random.normal(ks[2], (EDGE_DIM, D_IN), dtype=jnp.float32) / np.sqrt(EDGE_DIM)
        b_e = jax.random.normal(ks[3], (D_IN,), dtype=jnp.float32) * 0.01
        W_l = jax.random.normal(ks[4], (D_IN, D_OUT), dtype=jnp.float32) / np.sqrt(D_IN)
        b_l = jax.random.normal(ks[5], (D_OUT,), dtype=jnp.float32) * 0.01
        W_r = jax.random.normal(ks[6], (D_IN, D_OUT), dtype=jnp.float32) / np.sqrt(D_IN)
        edge_index = jax.random.randint(ks[7], (2, N_EDGES), 0, N_NODES, dtype=jnp.int64)
        return {'x': x, 'edge_attr': edge_attr, 'W_e': W_e, 'b_e': b_e, 'W_l': W_l, 'b_l': b_l, 'W_r': W_r, 'edge_index': edge_index}
    _L2_gnn_all = _L2_gnn_setup()
    _L2_gnn_in = {k: v for k, v in _L2_gnn_all.items() if k in ('W_e', 'b_e', 'W_l', 'b_l', 'W_r')}
    del _L2_gnn_all

    def _L3_gnn_setup():
        import jax, jax.numpy as jnp
        import numpy as np
        N_NODES = 6250
        N_EDGES = 200000
        IN_FEATS = 64
        RADIAL_FEATS = 128
        OUT_FEATS = 64

        def ssp(x):
            return jax.nn.softplus(x) - jnp.log(2.0).astype(x.dtype)
        key = jax.random.key(seed)
        ks = jax.random.split(key, 10)
        inp = {'node_h': jax.random.normal(ks[0], (N_NODES, IN_FEATS), dtype=jnp.float32), 'edge_h': jax.random.normal(ks[1], (N_EDGES, IN_FEATS), dtype=jnp.float32), 'bf': jax.random.uniform(ks[2], (N_EDGES, RADIAL_FEATS), dtype=jnp.float32), 'W1': jax.random.normal(ks[3], (RADIAL_FEATS, IN_FEATS), dtype=jnp.float32) / np.sqrt(RADIAL_FEATS), 'b1': jnp.zeros((IN_FEATS,), jnp.float32), 'W2': jax.random.normal(ks[4], (IN_FEATS, IN_FEATS), dtype=jnp.float32) / np.sqrt(IN_FEATS), 'b2': jnp.zeros((IN_FEATS,), jnp.float32), 'W3': jax.random.normal(ks[5], (IN_FEATS, OUT_FEATS), dtype=jnp.float32) / np.sqrt(IN_FEATS), 'b3': jnp.zeros((OUT_FEATS,), jnp.float32), 'W4': jax.random.normal(ks[6], (OUT_FEATS, IN_FEATS), dtype=jnp.float32) / np.sqrt(OUT_FEATS), 'b4': jnp.zeros((IN_FEATS,), jnp.float32), 'src': jax.random.randint(ks[7], (N_EDGES,), 0, N_NODES, dtype=jnp.int64 if jax.config.jax_enable_x64 else jnp.int32), 'dst': jax.random.randint(ks[8], (N_EDGES,), 0, N_NODES, dtype=jnp.int64 if jax.config.jax_enable_x64 else jnp.int32)}
        return inp
    _L3_gnn_all = _L3_gnn_setup()
    _L3_gnn_in = {k: v for k, v in _L3_gnn_all.items() if k in ('W1', 'b1', 'W2', 'b2', 'W3', 'b3', 'W4', 'b4')}
    del _L3_gnn_all
    return {'x': x, 'src': src, 'dst': dst, 'edge_attr_128': edge_attr_128, 'edge_attr_16': edge_attr_16, 'edge_attr_64': edge_attr_64, 'edge_type_3': edge_type_3, 'node_type_2': node_type_2, 'L0_gnn_W1': _L0_gnn_in['W1'], 'L0_gnn_b1': _L0_gnn_in['b1'], 'L0_gnn_W2': _L0_gnn_in['W2'], 'L0_gnn_b2': _L0_gnn_in['b2'], 'L0_gnn_W3': _L0_gnn_in['W3'], 'L0_gnn_b3': _L0_gnn_in['b3'], 'L0_gnn_W4': _L0_gnn_in['W4'], 'L0_gnn_b4': _L0_gnn_in['b4'], 'L0_gnn_W5': _L0_gnn_in['W5'], 'L0_gnn_b5': _L0_gnn_in['b5'], 'L1_gnn_w1_l': _L1_gnn_in['w1_l'], 'L1_gnn_b1': _L1_gnn_in['b1'], 'L1_gnn_w1_r': _L1_gnn_in['w1_r'], 'L1_gnn_w2_l': _L1_gnn_in['w2_l'], 'L1_gnn_b2': _L1_gnn_in['b2'], 'L1_gnn_w2_r': _L1_gnn_in['w2_r'], 'L2_gnn_W_e': _L2_gnn_in['W_e'], 'L2_gnn_b_e': _L2_gnn_in['b_e'], 'L2_gnn_W_l': _L2_gnn_in['W_l'], 'L2_gnn_b_l': _L2_gnn_in['b_l'], 'L2_gnn_W_r': _L2_gnn_in['W_r'], 'L3_gnn_W1': _L3_gnn_in['W1'], 'L3_gnn_b1': _L3_gnn_in['b1'], 'L3_gnn_W2': _L3_gnn_in['W2'], 'L3_gnn_b2': _L3_gnn_in['b2'], 'L3_gnn_W3': _L3_gnn_in['W3'], 'L3_gnn_b3': _L3_gnn_in['b3'], 'L3_gnn_W4': _L3_gnn_in['W4'], 'L3_gnn_b4': _L3_gnn_in['b4']}

def reference(x, src, dst, edge_attr_128, edge_attr_16, edge_attr_64, edge_type_3, node_type_2, L0_gnn_W1, L0_gnn_b1, L0_gnn_W2, L0_gnn_b2, L0_gnn_W3, L0_gnn_b3, L0_gnn_W4, L0_gnn_b4, L0_gnn_W5, L0_gnn_b5, L1_gnn_w1_l, L1_gnn_b1, L1_gnn_w1_r, L1_gnn_w2_l, L1_gnn_b2, L1_gnn_w2_r, L2_gnn_W_e, L2_gnn_b_e, L2_gnn_W_l, L2_gnn_b_l, L2_gnn_W_r, L3_gnn_W1, L3_gnn_b1, L3_gnn_W2, L3_gnn_b2, L3_gnn_W3, L3_gnn_b3, L3_gnn_W4, L3_gnn_b4):
    import jax
    import jax.numpy as jnp

    def _L0_gnn_ref(x, edge_feat, W1, b1, W2, b2, W3, b3, W4, b4, W5, b5, node_type, edge_src, edge_dst, edge_type):
        import jax, jax.numpy as jnp
        import numpy as np
        N, M = (12500, 100000)
        F_IN, F_E, H = (64, 16, 64)
        T_NODE, T_EDGE = (2, 3)
        HEAD_DIM = 16.0

        def _node_proj(x, W, b, node_type):
            p = jnp.einsum('nf,tfh->tnh', x, W) + b[:, None, :]
            return jnp.take_along_axis(p, node_type[None, :, None], axis=0)[0]
        n = x.shape[0]
        h1 = _node_proj(x, W1, b1, node_type)
        h2 = _node_proj(x, W2, b2, node_type)
        h3 = _node_proj(x, W3, b3, node_type)
        h4 = _node_proj(x, W4, b4, node_type)
        w5e = jnp.einsum('mf,mfh->mh', edge_feat, W5[edge_type]) + b5[edge_type]
        num = jnp.sum(h3[edge_dst] * (h4[edge_src] + w5e), axis=-1)
        score = jax.nn.softmax((num / jnp.sqrt(HEAD_DIM))[:, None], axis=-1)[:, 0]
        msg = score[:, None] * (h2[edge_src] + w5e)
        out = h1 + jax.ops.segment_sum(msg, edge_dst, num_segments=n)
        return out

    def _L1_gnn_ref(x, edge_index, w1_l, b1, w1_r, w2_l, b2, w2_r):
        import jax, jax.numpy as jnp
        import numpy as np
        N_NODES = 12500
        N_EDGES = 156250
        D_IN = 64
        D_HID = 64
        D_OUT = 64

        def sage_conv(x, edge_index, w_l, b_l, w_r):
            src, dst = (edge_index[0], edge_index[1])
            n = x.shape[0]
            msg_sum = jax.ops.segment_sum(x[src], dst, num_segments=n)
            deg = jax.ops.segment_sum(jnp.ones((src.shape[0],), x.dtype), dst, num_segments=n)
            mean = msg_sum / jnp.maximum(deg, 1.0)[:, None]
            return mean @ w_l + b_l + x @ w_r
        h = jax.nn.relu(sage_conv(x, edge_index, w1_l, b1, w1_r))
        return sage_conv(h, edge_index, w2_l, b2, w2_r)

    def _L2_gnn_ref(x, edge_attr, W_e, b_e, W_l, b_l, W_r, edge_index):
        import jax, jax.numpy as jnp
        import numpy as np
        N_NODES = 12500
        N_EDGES = 125000
        D_IN = 64
        EDGE_DIM = 16
        D_OUT = 64
        n = x.shape[0]
        src, dst = (edge_index[0], edge_index[1])
        msg = x[src] + (edge_attr @ W_e + b_e)
        agg = jax.ops.segment_sum(msg, dst, num_segments=n)
        cnt = jax.ops.segment_sum(jnp.ones((msg.shape[0], 1), msg.dtype), dst, num_segments=n)
        agg = agg / jnp.maximum(cnt, 1.0)
        return agg @ W_l + b_l + x @ W_r

    def _L3_gnn_ref(node_h, edge_h, bf, W1, b1, W2, b2, W3, b3, W4, b4, src, dst):
        import jax, jax.numpy as jnp
        import numpy as np
        N_NODES = 6250
        N_EDGES = 200000
        IN_FEATS = 64
        RADIAL_FEATS = 128
        OUT_FEATS = 64

        def ssp(x):
            return jax.nn.softplus(x) - jnp.log(2.0).astype(x.dtype)
        n_nodes = node_h.shape[0]
        w = ssp(bf @ W1 + b1)
        w = ssp(w @ W2 + b2)
        eh = w * edge_h
        m = node_h[src] * eh
        s = jax.ops.segment_sum(m, dst, num_segments=n_nodes)
        cnt = jax.ops.segment_sum(jnp.ones((m.shape[0],), m.dtype), dst, num_segments=n_nodes)
        h = s / jnp.maximum(cnt, 1.0)[:, None]
        out = ssp(h @ W3 + b3)
        return ssp(out @ W4 + b4)
    edge_index = jnp.stack([src, dst])
    x = _layernorm(x + _L0_gnn_ref(x, edge_attr_16, L0_gnn_W1, L0_gnn_b1, L0_gnn_W2, L0_gnn_b2, L0_gnn_W3, L0_gnn_b3, L0_gnn_W4, L0_gnn_b4, L0_gnn_W5, L0_gnn_b5, node_type_2, src, dst, edge_type_3), axis=-1)
    x = _layernorm(x + _L1_gnn_ref(x, edge_index, L1_gnn_w1_l, L1_gnn_b1, L1_gnn_w1_r, L1_gnn_w2_l, L1_gnn_b2, L1_gnn_w2_r), axis=-1)
    x = _layernorm(x + _L2_gnn_ref(x, edge_attr_16, L2_gnn_W_e, L2_gnn_b_e, L2_gnn_W_l, L2_gnn_b_l, L2_gnn_W_r, edge_index), axis=-1)
    x = _layernorm(x + _L3_gnn_ref(x, edge_attr_64, edge_attr_128, L3_gnn_W1, L3_gnn_b1, L3_gnn_W2, L3_gnn_b2, L3_gnn_W3, L3_gnn_b3, L3_gnn_W4, L3_gnn_b4, src, dst), axis=-1)
    return x

_drawn_inputs = setup_inputs


def setup_inputs(seed=0):
    import zlib

    import numpy as np

    out = dict(_drawn_inputs(seed))
    spreads = {'L3_gnn_b1': (0.0, 0.8),
     'L3_gnn_b2': (0.0, 2.0),
     'L3_gnn_b3': (0.0, 2.0),
     'L3_gnn_b4': (0.0, 0.8)}
    factors = {'edge_attr_128': 8.0,
     'edge_attr_64': 7.068,
     'L0_gnn_b1': 25.214,
     'L2_gnn_b_e': 6.165,
     'L2_gnn_b_l': 7.299,
     'L3_gnn_W1': 6.811,
     'L3_gnn_W2': 8.0,
     'L3_gnn_W3': 6.986}
    for name, (base, spread) in spreads.items():
        noise = np.random.default_rng([zlib.crc32(name.encode()), seed]).standard_normal(out[name].shape)
        drawn = base * np.exp(spread * noise) if base else spread * noise
        out[name] = jnp.asarray(drawn.astype(out[name].dtype))
    for name, factor in factors.items():
        out[name] = (out[name] * factor).astype(out[name].dtype)
    return out
```

```python
from contextlib import ExitStack

import concourse.bass as bass
from concourse import mybir

F32 = mybir.dt.float32
I32 = mybir.dt.int32
ALU = mybir.AluOpType
ACT = mybir.ActivationFunctionType
AX = mybir.AxisListType

N = 6250
E = 200000
H = 64
FE = 16
TE = 3
P = 128
WIN = (N + P - 1) // P
COLS = 8
GE = P * COLS
GROUPS = (E + GE - 1) // GE
SLOTS = 4
STEPS = GROUPS // SLOTS
assert GROUPS % SLOTS == 0 and GROUPS % 2 == 0
FT = TE * (FE + 1)
RW = H + FT
CH = 7
CHUNKS = WIN // CH
assert WIN % CH == 0
EPS = 1e-5
PASSES = 5
DMA = 16


def build(nc, x, ntype, ntype2, src, dst_cols, dst_rows, etype, ef, ea, bft,
          w_typed, b_typed, w_edge, w_sage1, w_sage2, w_econv, w_cf1, w_cf2, w_cf3, w_cf4,
          bias_rows, bias_cf1, bias_cf2, bias_cf3, out):
    ctx = ExitStack()
    with ctx:
        def sb(name, shape, dt=F32):
            return ctx.enter_context(nc.sbuf_tensor(name, shape, dt))

        def pb(name, shape):
            return ctx.enter_context(nc.psum_tensor(name, shape, F32))

        def sem(name):
            return ctx.enter_context(nc.semaphore(name))

        table = nc.dram_tensor("node_table", (WIN * P, H), F32).ap()
        table_v = table.rearrange("(w p) f -> p w f", p=P)
        windows_dram = nc.dram_tensor("window_bounds", (2, GROUPS), I32).ap()

        iota = sb("iota", [P, WIN * P])
        pid = sb("pid", [P, 1])
        ident = sb("ident", [P, P])
        wt_typed = sb("wt_typed", [P, 2 * H])
        bt_typed = sb("bt_typed", [2, 2 * H])
        wt_edge = sb("wt_edge", [FT, 2 * H])
        wt_sage1 = sb("wt_sage1", [P, H])
        wt_sage2 = sb("wt_sage2", [P, H])
        wt_econv = sb("wt_econv", [P, H])
        wt_cf1 = sb("wt_cf1", [P, H])
        wt_cf2 = sb("wt_cf2", [P, 2 * H])
        wt_cf3 = sb("wt_cf3", [H, H])
        wt_cf4 = sb("wt_cf4", [H, H])
        bt_rows = sb("bt_rows", [P, 4, H])
        bt_cf1 = sb("bt_cf1", [P, 1])
        bt_cf2 = sb("bt_cf2", [1, COLS * H])
        bt_cf3 = sb("bt_cf3", [H, 1])
        half = sb("half", [P, 1])
        ones_row = sb("ones_row", [1, P])

        dstf = sb("dstf", [P, GROUPS * COLS])
        dsti = sb("dsti", [P, GROUPS * COLS], I32)
        bounds = sb("bounds", [GROUPS // 2, 2, 2], I32)
        bound_row = sb("bound_row", [1, 2, GROUPS], I32)
        scan = sb("scan", [1, 2, GROUPS], I32)
        sched = sb("sched", [1, GROUPS, 4], I32)

        xs = sb("xs", [P, WIN, H])
        hs = sb("hs", [P, WIN, H])
        edge_term = sb("edge_term", [P, WIN, H])
        acc = sb("acc", [P, WIN, RW])
        masks = sb("masks", [P, 2, WIN])
        ntypei = sb("ntypei", [P, WIN], I32)
        mask_rows = sb("mask_rows", [2, WIN * P])
        mask_rowsi = mask_rows[:, :].bitcast(I32)
        rcount = sb("rcount", [P, WIN])
        var = sb("var", [P, WIN])
        cat = sb("cat", [P, CH, P])
        cat_mask = sb("cat_mask", [2, CH, P])
        cat_t = sb("cat_t", [P, CH * P])
        y = sb("y", [P, CH, H])
        y2 = sb("y2", [P, CH, H])
        row_sum = sb("row_sum", [P, CH])

        idx = sb("idx", [P, SLOTS, COLS], I32)
        rows = sb("rows", [P, SLOTS, COLS, RW])
        onehot = sb("onehot", [P, COLS, P])
        etype_s = sb("etype_s", [P, SLOTS, COLS], I32)
        ef_s = sb("ef_s", [P, SLOTS, COLS, FE])
        bf_s = sb("bf_s", [P, SLOTS, GE])
        dst_row = bf_s[0:GROUPS // 2, 0:2, :].bitcast(I32)
        act_a = bf_s[:, 0, 0:CH * P]
        act_r = bf_s[:, 1, 0:CH * P]
        hid_t = bf_s[0:H, 2, 0:CH * P]
        ea_s = sb("ea_s", [P, SLOTS, COLS * H])
        filt_a = sb("filt_a", [P, 512])
        filt_r = sb("filt_r", [P, 512])
        filt_h = sb("filt_h", [P, 512])
        gate_a = sb("gate_a", [P, 2, 512])
        gate_r = sb("gate_r", [P, 2, 512])

        ps_turn = pb("ps_turn", [P, 2, 512])
        ps_proj = pb("ps_proj", [P, 2, 512])
        ps_sum = pb("ps_sum", [P, 512])
        ps_f1 = pb("ps_f1", [P, 512])
        ps_f2 = pb("ps_f2", [P, 512])

        loaded = sem("loaded")
        dst_loaded = sem("dst_loaded")
        iota_done = sem("iota_done")
        bounds_ready = sem("bounds_ready")
        bounds_out = sem("bounds_out")
        bounds_back = sem("bounds_back")
        sched_ready = sem("sched_ready")
        const_ready = sem("const_ready")

        cat_ready = sem("cat_ready")
        turned = sem("turned")
        cat_t_ready = sem("cat_t_ready")
        projected = sem("projected")
        proj_read = sem("proj_read")
        hid_act = sem("hid_act")
        hid_ready = sem("hid_ready")
        out_projected = sem("out_projected")
        out_biased = sem("out_biased")
        out_act = sem("out_act")
        out_used = sem("out_used")
        var_ready = sem("var_ready")
        std_ready = sem("std_ready")
        rows_ready = sem("rows_ready")
        table_written = sem("table_written")
        stored = sem("stored")

        slot_free = [sem(f"slot_free{u}") for u in range(SLOTS)]
        idx_loaded = [sem(f"idx_loaded{u}") for u in range(SLOTS)]
        feat_loaded = [sem(f"feat_loaded{u}") for u in range(SLOTS)]
        bf_loaded = [sem(f"bf_loaded{u}") for u in range(SLOTS)]
        ea_loaded = [sem(f"ea_loaded{u}") for u in range(SLOTS)]
        gathered = [sem(f"gathered{u}") for u in range(SLOTS)]
        feat_ready = sem("feat_ready")
        msg_ready = sem("msg_ready")
        f1_done = sem("f1_done")
        f1_act = sem("f1_act")
        f1_ready = sem("f1_ready")
        f2_done = sem("f2_done")
        f2_act = sem("f2_act")
        onehot_ready = [sem(f"onehot_ready{p}") for p in range(PASSES)]
        pair_summed = [sem(f"pair_summed{p}") for p in range(PASSES)]
        acc_added = [sem(f"acc_added{p}") for p in range(PASSES)]

        def visits(eng, g):
            n = eng.value_load(sched[0:1, bass.ds(g, 1), 1:2].rearrange("a g c -> a (g c)"), min_val=1, max_val=WIN)
            before = eng.value_load(sched[0:1, bass.ds(g, 1), 2:3].rearrange("a g c -> a (g c)"), min_val=0,
                                    max_val=GROUPS * WIN)
            return n, before

        LOADS = [(wt_typed[0:H, :], w_typed[0]), (wt_typed[H:P, :], w_typed[1]), (bt_typed[:, :], b_typed),
                 (wt_edge[:, :], w_edge), (wt_sage1[:, :], w_sage1), (wt_sage2[:, :], w_sage2),
                 (wt_econv[:, :], w_econv), (wt_cf1[:, :], w_cf1), (wt_cf2[:, :], w_cf2), (wt_cf3[:, :], w_cf3), (wt_cf4[:, :], w_cf4),
                 (bt_rows[:, :, :], bias_rows), (bt_cf1[:, :], bias_cf1), (bt_cf2[:, :], bias_cf2),
                 (bt_cf3[:, :], bias_cf3), (xs[:, :, :], x), (ntypei[:, :], ntype), (mask_rowsi, ntype2)]

        block = ctx.enter_context(nc.Block())

        @block.sync
        def _(sp):
            sp.dma_start(dst_row[:, :, :], dst_rows).then_inc(dst_loaded, DMA)
            for to, of in LOADS:
                sp.dma_start(to, of).then_inc(loaded, DMA)
            sp.dma_start(dsti[:, :], dst_cols).then_inc(loaded, DMA)
            sp.wait_ge(bounds_ready, 1)
            sp.dma_start(windows_dram.rearrange("b (q t) -> q b t", t=2), bounds[:, :, :]).then_inc(bounds_out, DMA)
            sp.wait_ge(bounds_out, DMA)
            sp.dma_start(bound_row[0:1, :, :], windows_dram.unsqueeze(0)).then_inc(bounds_back, DMA)

            def write_table(p, rows_of):
                sp.wait_ge(rows_ready, p + 1)
                sp.dma_start(table_v, rows_of[:, :, :]).then_inc(table_written, DMA)

            def load_groups(p):
                with sp.Fori(0, STEPS) as i:
                    for u in range(SLOTS):
                        g = i * SLOTS + u
                        sp.wait_ge(slot_free[u], i + (p * STEPS + 1))
                        sp.dma_start(idx[:, u, :], src[bass.ds(g, 1)].squeeze(0)).then_inc(idx_loaded[u], DMA)
                        if p == 0:
                            sp.dma_start(etype_s[:, u, :], etype[bass.ds(g, 1)].squeeze(0)).then_inc(feat_loaded[u], DMA)
                            sp.dma_start(ef_s[:, u, :, :].rearrange("p c f -> p (c f)"),
                                         ef[bass.ds(g, 1)].squeeze(0)).then_inc(feat_loaded[u], DMA)
                        if p == PASSES - 1:
                            sp.dma_start(bf_s[:, u, :], bft[bass.ds(g, 1)].squeeze(0)).then_inc(bf_loaded[u], DMA)
                            sp.dma_start(ea_s[:, u, :], ea[bass.ds(g, 1)].squeeze(0)).then_inc(ea_loaded[u], DMA)

            for p in range(PASSES):
                write_table(p, hs if p in (0, 2) else xs)
                load_groups(p)
            sp.wait_ge(rows_ready, PASSES + 1)
            full = N // P
            sp.dma_start(out[0:full * P, :].rearrange("(w p) f -> p w f", p=P), xs[:, 0:full, :]).then_inc(stored, DMA)
            sp.dma_start(out[full * P:N, :], xs[0:N - full * P, full, :]).then_inc(stored, DMA)
            sp.wait_ge(stored, 2 * DMA)

        @block.gpsimd
        def _(pool):
            pool.iota(iota[:, :], [[1, WIN * P]], base=0, channel_multiplier=0,
                      allow_small_or_imprecise_dtypes=True).then_inc(iota_done, 1)
            pool.iota(pid[:, :], [[0, 1]], base=0, channel_multiplier=1,
                      allow_small_or_imprecise_dtypes=True).then_inc(iota_done, 1)
            for p in range(PASSES):
                pool.wait_ge(table_written, (p + 1) * DMA)
                with pool.Fori(0, STEPS) as i:
                    for u in range(SLOTS):
                        pool.wait_ge(idx_loaded[u], (i + (p * STEPS + 1)) * DMA)
                        pool.nop(nofuse=True)
                        for c in range(COLS):
                            pool.indirect_dma_start(
                                rows[:, u, c, 0:H], None, table,
                                bass.IndirectOffsetOnAxis(ap=idx[:, u, c:c + 1], axis=0)).then_inc(gathered[u], DMA)

        @block.tensor
        def _(pe):
            def node_phase(ph, kin, project):
                with pe.Fori(0, CHUNKS) as c:
                    pe.wait_ge(cat_ready, c + (ph * CHUNKS + 1))
                    pe.nop(nofuse=True)
                    for j in range(CH):
                        last = pe.transpose(ps_turn[0:kin, j // 4, (j % 4) * P:(j % 4 + 1) * P], cat[:, j, 0:kin],
                                            ident[:, :])
                    last.then_inc(turned, 1)
                    pe.wait_ge(cat_t_ready, c + (ph * CHUNKS + 1))
                    pe.wait_ge(proj_read, c + (ph * CHUNKS + 1))
                    pe.nop(nofuse=True)
                    project(c)

            def project_rows(kin, wt, width, bias_of_type=False):
                def go(c):
                    per = 512 // width
                    for j in range(CH):
                        o = ps_proj[:, j // per, (j % per) * width:(j % per + 1) * width]
                        last = pe.matmul(o, cat_t[0:kin, j * P:(j + 1) * P], wt, start=True, stop=not bias_of_type)
                        if bias_of_type:
                            last = pe.matmul(o, cat_mask[:, j, :], bt_typed[:, :], start=False, stop=True)
                    last.then_inc(projected, 1)
                return go

            def project_cf(c):
                pe.matmul(ps_proj[0:H, 0, :], wt_cf3[:, :], cat_t[0:H, 0:512], start=True, stop=True)
                pe.matmul(ps_proj[0:H, 1, 0:CH * P - 512], wt_cf3[:, :], cat_t[0:H, 512:CH * P], start=True,
                          stop=True).then_inc(projected, 1)
                pe.wait_ge(hid_ready, c + 1)
                pe.nop(nofuse=True)
                for j in range(CH):
                    last = pe.matmul(ps_f2[:, j * H:(j + 1) * H], hid_t[:, j * P:(j + 1) * P], wt_cf4[:, :],
                                     start=True, stop=True)
                last.then_inc(out_projected, 1)

            def sum_group(p, u, g, width):
                n, before = visits(pe, g)
                with pe.Fori(0, n) as k:
                    pe.wait_ge(acc_added[p], before + k + 1)
                    for c in range(COLS):
                        if c % 4 == 0:
                            pe.wait_ge(onehot_ready[p], (before + k) * 2 + (c // 4 + 1))
                        last = pe.matmul(ps_sum[:, 0:width], onehot[:, c, :], rows[:, u, c, 0:width],
                                         start=(c == 0), stop=(c == COLS - 1))
                    last.then_inc(pair_summed[p], 1)

            def plain_pass(p, width):
                with pe.Fori(0, STEPS) as i:
                    for u in range(SLOTS):
                        g = i * SLOTS + u
                        pe.wait_ge(gathered[u], (i + (p * STEPS + 1)) * (COLS * DMA))
                        if p == 0:
                            pe.wait_ge(feat_ready, g + 1)
                        sum_group(p, u, g, width)

            def filter1(i, u, g):
                pe.wait_ge(bf_loaded[u], (i + 1) * DMA)
                pe.wait_ge(f1_ready, g)
                for s in range(2):
                    last = pe.matmul(ps_f1[s * H:(s + 1) * H, :], wt_cf1[:, :], bf_s[:, u, s * 512:(s + 1) * 512],
                                     start=True, stop=True)
                last.then_inc(f1_done, 1)

            def filter2(g):
                pe.wait_ge(f1_ready, g + 2)
                pe.wait_ge(f2_act, g + 1)
                pe.matmul(ps_f2[:, :], ones_row[0:1, :], bt_cf2[0:1, :], start=True, stop=False)
                for q in range(COLS // 2):
                    last = pe.matmul(ps_f2[:, q * 2 * H:(q + 1) * 2 * H], filt_h[:, q * P:(q + 1) * P], wt_cf2[:, :],
                                     start=False, stop=(q == COLS // 2 - 1))
                last.then_inc(f2_done, 1)

            pe.wait_ge(const_ready, 1)
            pe.wait_ge(loaded, (len(LOADS) + 1) * DMA)
            node_phase(0, P, project_rows(P, wt_typed[:, :], 2 * H, bias_of_type=True))
            pe.wait_ge(sched_ready, 1)
            plain_pass(0, RW)
            node_phase(1, FT, project_rows(FT, wt_edge[:, :], 2 * H))
            plain_pass(1, H)
            node_phase(2, P, project_rows(P, wt_sage1[:, :], H))
            plain_pass(2, H)
            node_phase(3, P, project_rows(P, wt_sage2[:, :], H))
            plain_pass(3, H)
            node_phase(4, P, project_rows(P, wt_econv[:, :], H))

            def cf_steps(i, first=False, last=False):
                for u in range(SLOTS):
                    g = i * SLOTS + u
                    filter2(g)
                    if not (last and u == SLOTS - 1):
                        up = (u + 1) % SLOTS
                        filter1(i + (u + 1) // SLOTS, up, g + 1)
                    if not (first and u == 0):
                        pe.wait_ge(msg_ready, g)
                        sum_group(PASSES - 1, (u - 1) % SLOTS, g - 1, H)

            pe.wait_ge(bf_loaded[0], DMA)
            for s in range(2):
                last = pe.matmul(ps_f1[s * H:(s + 1) * H, :], wt_cf1[:, :], bf_s[:, 0, s * 512:(s + 1) * 512],
                                 start=True, stop=True)
            last.then_inc(f1_done, 1)
            cf_steps(0, first=True)
            with pe.Fori(1, STEPS - 1) as i:
                cf_steps(i)
            cf_steps(STEPS - 1, last=True)
            pe.wait_ge(msg_ready, GROUPS)
            sum_group(PASSES - 1, SLOTS - 1, GROUPS - 1, H)
            node_phase(5, H, project_cf)

        @block.scalar
        def _(act):
            def ssp_terms(src_ap, a, r, bias, done, step):
                act.activation(a, src_ap, ACT.Abs, bias=bias)
                act.activation(r, src_ap, ACT.Relu, bias=bias)
                act.drain()
                act.activation(a, a, ACT.Exp, scale=-1.0)
                act.drain()
                act.activation(a, a, ACT.Ln, scale=0.5, bias=half[0:a.shape[0], :]).then_inc(done, 1)

            def node_phase(ph, kin, cf=False):
                with act.Fori(0, CHUNKS) as c:
                    act.wait_ge(turned, c + (ph * CHUNKS + 1))
                    act.activation(cat_t[0:kin, 0:512], ps_turn[0:kin, 0, :], ACT.Copy)
                    act.activation(cat_t[0:kin, 512:CH * P], ps_turn[0:kin, 1, 0:CH * P - 512],
                                   ACT.Copy).then_inc(cat_t_ready, 1)
                    if cf:
                        act.wait_ge(projected, c + (ph * CHUNKS + 1))
                        act.wait_ge(out_used, c + 1)
                        n = CH * P
                        act.activation(act_a[0:H, 0:512], ps_proj[0:H, 0, :], ACT.Abs, bias=bt_cf3[:, :])
                        act.activation(act_a[0:H, 512:n], ps_proj[0:H, 1, 0:n - 512], ACT.Abs, bias=bt_cf3[:, :])
                        act.activation(act_r[0:H, 0:512], ps_proj[0:H, 0, :], ACT.Relu, bias=bt_cf3[:, :])
                        act.activation(act_r[0:H, 512:n], ps_proj[0:H, 1, 0:n - 512], ACT.Relu, bias=bt_cf3[:, :])
                        act.drain()
                        act.activation(act_a[0:H, :], act_a[0:H, :], ACT.Exp, scale=-1.0)
                        act.drain()
                        act.activation(act_a[0:H, :], act_a[0:H, :], ACT.Ln, scale=0.5,
                                       bias=half[0:H, :]).then_inc(hid_act, 1)
                        act.wait_ge(out_biased, c + 1)
                        m = CH * H
                        yv = y2[:, :, :].rearrange("p j f -> p (j f)")
                        act.activation(act_a[:, 0:m], yv, ACT.Abs)
                        act.activation(act_r[:, 0:m], yv, ACT.Relu)
                        act.drain()
                        act.activation(act_a[:, 0:m], act_a[:, 0:m], ACT.Exp, scale=-1.0)
                        act.drain()
                        act.activation(act_a[:, 0:m], act_a[:, 0:m], ACT.Ln, scale=0.5,
                                       bias=half[:, :]).then_inc(out_act, 1)

            norms = [0]

            def deviations():
                norms[0] += 1
                act.wait_ge(var_ready, norms[0])
                act.activation(var[:, :], var[:, :], ACT.Sqrt).then_inc(std_ready, 1)

            act.wait_ge(const_ready, 1)
            act.wait_ge(loaded, (len(LOADS) + 1) * DMA)
            node_phase(0, P)
            node_phase(1, FT)
            deviations()
            node_phase(2, P)
            node_phase(3, P)
            deviations()
            node_phase(4, P)
            deviations()
            def cf_act(g):
                act.wait_ge(f1_done, g + 1)
                act.wait_ge(f1_ready, g + 1)
                ssp_terms(ps_f1[:, :], filt_a[:, :], filt_r[:, :], bt_cf1[:, :], f1_act, 1)

            def cf_gate(g, u):
                act.wait_ge(f2_done, g + 1)
                a, r = gate_a[:, u % 2, :], gate_r[:, u % 2, :]
                act.activation(a, ps_f2[:, :], ACT.Abs)
                act.activation(r, ps_f2[:, :], ACT.Relu)
                act.drain()
                act.activation(a, a, ACT.Exp, scale=-1.0)
                act.drain()
                act.activation(a, a, ACT.Ln, scale=0.5, bias=half[:, :]).then_inc(f2_act, 1)

            def cf_steps(i, last=False):
                for u in range(SLOTS):
                    g = i * SLOTS + u
                    cf_gate(g, u)
                    if not (last and u == SLOTS - 1):
                        cf_act(g + 1)

            cf_act(0)
            with act.Fori(0, STEPS - 1) as i:
                cf_steps(i)
            cf_steps(STEPS - 1, last=True)
            node_phase(5, H, cf=True)
            deviations()

        @block.vector
        def _(dve):
            def w3(t, c, a=0, b=H):
                return t[:, bass.ds(c * CH, CH), a:b]

            def per_row(t, c):
                return t[:, bass.ds(c * CH, CH)].unsqueeze(2).to_broadcast([P, CH, H])

            def proj(width, a, b):
                per = 512 // width
                for k in range(0, CH, per):
                    m = min(per, CH - k)
                    yield k, m, ps_proj[:, k // per, 0:m * width].rearrange("p (j f) -> p j f", f=width)[:, :, a:b]

            def center(c):
                dve.drain()
                dve.tensor_reduce(row_sum[:, :], y[:, :, :], axis=AX.X, op=ALU.add)
                dve.drain()
                dve.tensor_scalar(row_sum[:, :], row_sum[:, :], 1.0 / H, None, ALU.mult)
                dve.drain()
                dve.tensor_tensor(w3(xs, c), y[:, :, :], row_sum[:, :].unsqueeze(2).to_broadcast([P, CH, H]), ALU.subtract)
                dve.drain()
                dve.tensor_tensor(y[:, :, :], w3(xs, c), w3(xs, c), ALU.mult)
                dve.drain()
                dve.tensor_reduce(row_sum[:, :], y[:, :, :], axis=AX.X, op=ALU.add)
                dve.drain()
                dve.tensor_scalar(var[:, bass.ds(c * CH, CH)], row_sum[:, :], 1.0 / H, EPS, ALU.mult, ALU.add)

            norms = [0]

            def normalize():
                norms[0] += 1
                dve.drain().then_inc(var_ready, 1)
                dve.wait_ge(std_ready, norms[0])
                dve.reciprocal(var[:, :], var[:, :])
                dve.drain()
                dve.tensor_tensor(xs[:, :, :], xs[:, :, :], var[:, :].unsqueeze(2).to_broadcast([P, WIN, H]),
                                  ALU.mult).then_inc(rows_ready, 1)

            def node_phase(ph, build_cat, post):
                build_cat(0)
                with dve.Fori(0, CHUNKS - 1) as c:
                    dve.wait_ge(projected, c + (ph * CHUNKS + 1))
                    build_cat(c + 1)
                    post(c)
                    dve.drain()
                dve.wait_ge(projected, (ph + 1) * CHUNKS)
                post(CHUNKS - 1)

            def sum_group(p, g, width):
                first = dve.value_load(sched[0:1, bass.ds(g, 1), 0:1].rearrange("a g c -> a (g c)"), min_val=0,
                                       max_val=WIN - 1)
                n, before = visits(dve, g)
                with dve.Fori(0, n) as k:
                    w = nc.s_assert_within(first + k, 0, WIN - 1, skip_runtime_bounds_check_because=
                                           "a group's windows end at that of its greatest destination")
                    for c in range(COLS):
                        last = dve.tensor_scalar(onehot[:, c, :], iota[:, bass.ds(w * P, P)],
                                                 dstf[:, bass.ds(g * COLS + c, 1)], None, ALU.is_equal)
                        if c % 4 == 3:
                            last.then_inc(onehot_ready[p], 1)
                    dve.wait_ge(pair_summed[p], before + k + 1)
                    dve.wait_ge(acc_added[p], before + k + 1)
                    a = acc[:, bass.ds(w, 1), 0:width]
                    dve.tensor_tensor(a, a, ps_sum[:, 0:width].unsqueeze(1), ALU.add).then_inc(acc_added[p], 1)

            def clear(p, width):
                dve.drain()
                dve.memset(acc[:, :, 0:width], 0.0).then_inc(acc_added[p], 1)

            def edge_features(i, u, g):
                dve.wait_ge(feat_loaded[u], (i + 1) * (2 * DMA))
                for t in range(TE):
                    at = H + t * (FE + 1)
                    dve.scalar_tensor_tensor(rows[:, u, :, at:at + FE],
                                             etype_s[:, u, :].unsqueeze(2).to_broadcast([P, COLS, FE]), float(t),
                                             ef_s[:, u, :, :], ALU.is_equal, ALU.mult)
                    last = dve.tensor_scalar(rows[:, u, :, at + FE:at + FE + 1], etype_s[:, u, :].unsqueeze(2),
                                             float(t), None, ALU.is_equal)
                last.then_inc(feat_ready, 1)

            def plain_pass(p, width):
                clear(p, width)
                with dve.Fori(0, STEPS) as i:
                    for u in range(SLOTS):
                        g = i * SLOTS + u
                        if p == 0:
                            edge_features(i, u, g)
                        sum_group(p, g, width)
                        dve.sem_inc(slot_free[u], 1)

            dve.memset(half[:, :], 0.5)
            dve.memset(ones_row[:, :], 1.0)
            for u in range(SLOTS):
                dve.sem_inc(slot_free[u], 1)
            dve.sem_inc(proj_read, 1)
            dve.wait_ge(iota_done, 2)
            dve.tensor_scalar(ident[:, :], iota[:, 0:P], pid[:, 0:1], None, ALU.is_equal)
            dve.drain().then_inc(const_ready, 1)

            dve.wait_ge(dst_loaded, DMA)
            for b, op in enumerate((ALU.min, ALU.max)):
                dve.tensor_reduce(bounds[:, b, :], dst_row[:, :, :], axis=AX.X, op=op)
            dve.drain()
            dve.tensor_scalar(bounds[:, :, :], bounds[:, :, :], P.bit_length() - 1, None,
                              ALU.arith_shift_right).then_inc(bounds_ready, 1)

            dve.wait_ge(loaded, (len(LOADS) + 1) * DMA)
            for t in range(2):
                dve.tensor_scalar(masks[:, t, :], ntypei[:, :], float(t), None, ALU.is_equal)
            dve.tensor_scalar(mask_rows[:, :], mask_rowsi, pid[0:2, 0:1], None, ALU.is_equal)
            dve.tensor_copy(dstf[:, :], dsti[:, :])
            dve.drain()

            def cat_typed(c):
                for t in range(2):
                    dve.tensor_tensor(cat[:, :, t * H:(t + 1) * H], w3(xs, c),
                                      masks[:, t, bass.ds(c * CH, CH)].unsqueeze(2).to_broadcast([P, CH, H]), ALU.mult)
                dve.tensor_copy(cat_mask[:, :, :].rearrange("t j p -> t (j p)"),
                                mask_rows[:, bass.ds(c * (CH * P), CH * P)]).then_inc(cat_ready, 1)

            def post_typed(c):
                for k, m, v in proj(2 * H, 0, H):
                    dve.tensor_copy(hs[:, bass.ds(c * CH + k, m), :], v)
                for k, m, v in proj(2 * H, H, 2 * H):
                    xv = xs[:, bass.ds(c * CH + k, m), :]
                    last = dve.tensor_tensor(xv, xv, v, ALU.add)
                last.then_inc(proj_read, 1)

            node_phase(0, cat_typed, post_typed)
            dve.drain().then_inc(rows_ready, 1)

            dve.wait_ge(bounds_back, DMA)
            dve.tensor_tensor(scan[:, 0, :], bound_row[:, 1, :], bound_row[:, 0, :], ALU.subtract)
            dve.drain()
            dve.tensor_scalar(scan[:, 0, :], scan[:, 0, :], 1.0, None, ALU.add)
            dve.drain()
            dve.tensor_copy(sched[:, :, 0], bound_row[:, 0, :])
            dve.tensor_copy(sched[:, :, 1], scan[:, 0, :])
            s, at = 1, 0
            while s < GROUPS:
                dve.drain()
                dve.tensor_copy(scan[:, 1 - at, 0:s], scan[:, at, 0:s])
                dve.tensor_tensor(scan[:, 1 - at, s:], scan[:, at, s:], scan[:, at, 0:GROUPS - s], ALU.add)
                s, at = 2 * s, 1 - at
            dve.drain()
            dve.tensor_tensor(sched[:, :, 2], scan[:, at, :], sched[:, :, 1], ALU.subtract)
            dve.drain().then_inc(sched_ready, 1)

            plain_pass(0, RW)

            def cat_edge(c):
                dve.tensor_copy(cat[:, :, 0:FT], w3(acc, c, H, RW))
                last_of = w3(acc, c, H, RW).rearrange("p w (t k) -> p w t k", t=TE)[:, :, :, FE]
                dve.tensor_reduce(row_sum[:, :], last_of, axis=AX.X, op=ALU.add)
                dve.drain()
                rc = rcount[:, bass.ds(c * CH, CH)]
                dve.tensor_scalar(rc, row_sum[:, :], 1.0, None, ALU.max)
                dve.drain()
                dve.reciprocal(rc, rc).then_inc(cat_ready, 1)

            def post_edge(c):
                for k, m, v in proj(2 * H, 0, H):
                    dve.tensor_tensor(y[:, k:k + m, :], w3(acc, c)[:, k:k + m, :], v, ALU.add)
                for k, m, v in proj(2 * H, H, 2 * H):
                    last = dve.tensor_copy(edge_term[:, bass.ds(c * CH + k, m), :], v)
                last.then_inc(proj_read, 1)
                dve.drain()
                dve.tensor_tensor(y[:, :, :], y[:, :, :], w3(xs, c), ALU.add)
                center(c)

            dve.drain()
            node_phase(1, cat_edge, post_edge)
            normalize()

            def cat_mean(other, term=None):
                def go(c):
                    if term is not None:
                        dve.tensor_tensor(w3(acc, c), w3(acc, c), w3(term, c), ALU.add)
                        dve.drain()
                    dve.tensor_tensor(cat[:, :, 0:H], w3(acc, c), per_row(rcount, c), ALU.mult)
                    dve.tensor_copy(cat[:, :, H:P], w3(other, c)).then_inc(cat_ready, 1)
                return go

            def biased(c, b):
                for k, m, v in proj(H, 0, H):
                    dve.tensor_tensor(y[:, k:k + m, :], v, bt_rows[:, b:b + 1, :].to_broadcast([P, m, H]),
                                      ALU.add).then_inc(proj_read, 1)
                dve.drain()

            def post_hidden(c):
                biased(c, 0)
                dve.tensor_scalar(w3(hs, c), y[:, :, :], 0.0, None, ALU.max)

            def post_layer(b):
                def go(c):
                    biased(c, b)
                    dve.tensor_tensor(y[:, :, :], y[:, :, :], w3(xs, c), ALU.add)
                    center(c)
                return go

            plain_pass(1, H)
            dve.drain()
            node_phase(2, cat_mean(xs), post_hidden)
            dve.drain().then_inc(rows_ready, 1)
            plain_pass(2, H)
            dve.drain()
            node_phase(3, cat_mean(hs), post_layer(1))
            normalize()

            plain_pass(3, H)
            dve.drain()
            node_phase(4, cat_mean(xs, edge_term), post_layer(2))
            normalize()

            def hidden(g):
                dve.wait_ge(f1_act, g + 1)
                dve.wait_ge(f2_done, g) if not isinstance(g, int) or g > 0 else None
                dve.tensor_tensor(filt_h[:, :], filt_a[:, :], filt_r[:, :], ALU.add).then_inc(f1_ready, 1)

            def messages(i, u, g):
                a, r = gate_a[:, u % 2, :], gate_r[:, u % 2, :]
                dve.wait_ge(f2_act, g + 2)
                dve.tensor_tensor(r, r, a, ALU.add)
                dve.drain()
                dve.wait_ge(ea_loaded[u], (i + 1) * DMA)
                dve.tensor_tensor(r, r, ea_s[:, u, :], ALU.mult)
                dve.drain()
                dve.wait_ge(gathered[u], (i + ((PASSES - 1) * STEPS + 1)) * (COLS * DMA))
                dve.tensor_tensor(rows[:, u, :, 0:H], rows[:, u, :, 0:H], r.rearrange("p (c f) -> p c f", f=H),
                                  ALU.mult).then_inc(msg_ready, 1)

            def cf_steps(i, first=False, last=False):
                for u in range(SLOTS):
                    g = i * SLOTS + u
                    if not (first and u == 0):
                        up = (u - 1) % SLOTS
                        messages(i - (u == 0), up, g - 1)
                        sum_group(PASSES - 1, g - 1, H)
                        dve.sem_inc(slot_free[up], 1)
                    if not (last and u == SLOTS - 1):
                        hidden(g + 1)

            clear(PASSES - 1, H)
            dve.sem_inc(f1_ready, 1)
            dve.sem_inc(f2_act, 1)
            hidden(0)
            cf_steps(0, first=True)
            with dve.Fori(1, STEPS - 1) as i:
                cf_steps(i)
            cf_steps(STEPS - 1, last=True)
            messages(STEPS - 1, SLOTS - 1, GROUPS - 1)
            sum_group(PASSES - 1, GROUPS - 1, H)
            dve.drain()

            def cat_cf(c):
                dve.tensor_tensor(cat[:, :, 0:H], w3(acc, c), per_row(rcount, c), ALU.mult).then_inc(cat_ready, 1)

            def post_cf(c):
                dve.wait_ge(hid_act, c + 1)
                dve.tensor_tensor(hid_t[:, :], act_a[0:H, :], act_r[0:H, :], ALU.add).then_inc(hid_ready, 1)
                dve.wait_ge(out_projected, c + 1)
                dve.tensor_tensor(y2[:, :, :], ps_f2[:, 0:CH * H].rearrange("p (j f) -> p j f", f=H),
                                  bt_rows[:, 3:4, :].to_broadcast([P, CH, H]), ALU.add).then_inc(out_biased, 1)
                dve.wait_ge(out_act, c + 1)
                dve.sem_inc(proj_read, 1)
                av, rv = (t[:, 0:CH * H].rearrange("p (j f) -> p j f", f=H) for t in (act_a, act_r))
                dve.tensor_tensor(y[:, :, :], av, rv, ALU.add).then_inc(out_used, 1)
                dve.drain()
                dve.tensor_tensor(y[:, :, :], y[:, :, :], w3(xs, c), ALU.add)
                center(c)

            dve.sem_inc(out_used, 1)
            node_phase(5, cat_cf, post_cf)
            normalize()


_OUT = (N, H)


def kernel(x, src, dst, edge_attr_128, edge_attr_16, edge_attr_64, edge_type_3, node_type_2, L0_gnn_W1, L0_gnn_b1,
           L0_gnn_W2, L0_gnn_b2, L0_gnn_W3, L0_gnn_b3, L0_gnn_W4, L0_gnn_b4, L0_gnn_W5, L0_gnn_b5, L1_gnn_w1_l,
           L1_gnn_b1, L1_gnn_w1_r, L1_gnn_w2_l, L1_gnn_b2, L1_gnn_w2_r, L2_gnn_W_e, L2_gnn_b_e, L2_gnn_W_l,
           L2_gnn_b_l, L2_gnn_W_r, L3_gnn_W1, L3_gnn_b1, L3_gnn_W2, L3_gnn_b2, L3_gnn_W3, L3_gnn_b3, L3_gnn_W4,
           L3_gnn_b4):
    import numpy as np
    import concourse.bacc as bacc
    from concourse.bass_utils import run_bass_kernel_spmd as run

    a = np.asarray
    EP, NP = GROUPS * GE, WIN * P

    def edges(v, fill=0):
        v = a(v)
        return np.concatenate([v, np.full((EP - E,) + v.shape[1:], fill, v.dtype)])

    def nodes(v):
        v = a(v)
        return np.concatenate([v, np.zeros((NP - N,) + v.shape[1:], v.dtype)])

    dst_p = edges(dst, NP - 1)
    nt = nodes(node_type_2)
    W5, b5, We, be = a(L0_gnn_W5), a(L0_gnn_b5), a(L2_gnn_W_e), a(L2_gnn_b_e)
    W2, zero = a(L3_gnn_W2), np.zeros((H, H), np.float32)
    w_edge = np.concatenate([np.concatenate([np.concatenate([W5[t], b5[t][None]]), np.concatenate([We, be[None]])], 1)
                             for t in range(TE)])
    arrays = {
        "x": nodes(x).reshape(WIN, P, H).transpose(1, 0, 2),
        "ntype": nt.reshape(WIN, P).T,
        "ntype2": np.stack([nt, nt]),
        "src": edges(src).reshape(GROUPS, P, COLS),
        "dst_cols": dst_p.reshape(GROUPS, P, COLS).transpose(1, 0, 2).reshape(P, GROUPS * COLS),
        "dst_rows": dst_p.reshape(GROUPS // 2, 2, GE),
        "etype": edges(edge_type_3).reshape(GROUPS, P, COLS),
        "ef": edges(edge_attr_16).reshape(GROUPS, P, COLS * FE),
        "ea": edges(edge_attr_64).reshape(GROUPS, P, COLS * H),
        "bft": edges(edge_attr_128).reshape(GROUPS, P, COLS // 2, 2, P).transpose(0, 4, 3, 2, 1).reshape(GROUPS, P, GE),
        "w_typed": np.concatenate([a(L0_gnn_W2), a(L0_gnn_W1)], 2),
        "b_typed": np.concatenate([a(L0_gnn_b2), a(L0_gnn_b1)], 1),
        "w_edge": w_edge,
        "w_sage1": np.concatenate([a(L1_gnn_w1_l), a(L1_gnn_w1_r)]),
        "w_sage2": np.concatenate([a(L1_gnn_w2_l), a(L1_gnn_w2_r)]),
        "w_econv": np.concatenate([a(L2_gnn_W_l), a(L2_gnn_W_r)]),
        "w_cf1": a(L3_gnn_W1), "w_cf2": np.block([[W2, zero], [zero, W2]]), "w_cf3": a(L3_gnn_W3), "w_cf4": a(L3_gnn_W4),
        "bias_rows": np.stack([np.broadcast_to(a(b), (P, H)) for b in (L1_gnn_b1, L1_gnn_b2, L2_gnn_b_l, L3_gnn_b4)], 1),
        "bias_cf1": np.concatenate([a(L3_gnn_b1)] * 2)[:, None],
        "bias_cf2": np.concatenate([a(L3_gnn_b2)] * COLS)[None],
        "bias_cf3": a(L3_gnn_b3)[:, None],
    }
    arrays = {f"in_{n}": np.ascontiguousarray(v) for n, v in arrays.items()}
    nc = bacc.Bacc("TRN2", target_bir_lowering=False, num_devices=1)
    args = [nc.dram_tensor(n, v.shape, mybir.dt.from_np(v.dtype), kind="ExternalInput").ap() for n, v in arrays.items()]
    out = nc.dram_tensor("out_nodes", _OUT, F32, kind="ExternalOutput").ap()
    build(nc, *args, out)
    return run(nc, [arrays], core_ids=[0]).results[0]["out_nodes"]
```
